# Optimizing a Trainium2 kernel written in Bass

```python
import numpy as np
import jax
import jax.numpy as jnp

def _softmax(x, axis=-1):
    return jax.nn.softmax(x, axis=axis)

def _gelu(x):
    return jax.nn.gelu(x, approximate=True)

def _silu(x):
    return jax.nn.silu(x)

def _sigmoid(x):
    return jax.nn.sigmoid(x)

def _layernorm(x, axis=-1, eps=1e-05):
    m = jnp.mean(x, axis=axis, keepdims=True)
    v = jnp.var(x, axis=axis, keepdims=True)
    return (x - m) / jnp.sqrt(v + eps)

def _scatter_add(tgt, idx, src, axis=0):
    return tgt.at[idx].add(src)

def _segment_sum(src, seg, n):
    return jax.ops.segment_sum(src, seg, n)
kernel_name = 'mk_adj_preln_d2_adj_r2_287347'

def setup_inputs(seed: int=0):
    np.random.seed(seed)
    _w = jnp.asarray

    def _rec_inputs():
        import jax
        import jax.numpy as jnp
        _gk = jax.random.key(seed)
        x = -0.0005207 + 1.001 * jax.random.normal(jax.random.fold_in(_gk, 1), (4096, 128), jnp.float32)
        _w = (1.0 + jnp.arange(4096, dtype=jnp.float32)) ** (-0.5)
        _w = _w / _w.mean()
        _pij = jnp.clip(0.000488281 * _w[:, None] * _w[None, :], 0.0, 1.0)
        _a = jax.random.uniform(jax.random.fold_in(_gk, 2), (4096, 4096)) < _pij
        _af = _a.astype(jnp.float32)
        adj = _af
        return (x, adj)
    x, adj = _rec_inputs()

    def _L0_gnn_setup():
        import jax, jax.numpy as jnp
        import numpy as np
        NEG_INF = -9000000000000000.0
        NEG_SLOPE = 0.2
        key = jax.random.key(seed)
        k1, k2, k3, k4 = jax.random.split(key, 4)
        N, d_in, d_out = (4096, 128, 128)
        x = jax.random.normal(k1, (N, d_in), dtype=jnp.float32)
        adj = jax.random.randint(k2, (N, N), 0, 2).astype(jnp.float32)
        W = jax.random.normal(k3, (d_in, d_out), dtype=jnp.float32) * (1.0 / np.sqrt(d_in))
        a = jax.random.normal(k4, (2 * d_out,), dtype=jnp.float32) * (1.0 / np.sqrt(2 * d_out))
        return {'x': x, 'adj': adj, 'W': W, 'a': a}
    _L0_gnn_all = _L0_gnn_setup()
    _L0_gnn_in = {k: v for k, v in _L0_gnn_all.items() if k in ('W', 'a')}
    del _L0_gnn_all

    def _L1_gnn_setup():
        import jax, jax.numpy as jnp
        import numpy as np
        N = 4096
        D = 128
        CUTOFF = 1.0
        MU = 1.0
        SIGMA = 0.5

        def sensitivity(r, mu, sigma):
            return jnp.exp(-(1.0 / r - 1.0 / mu) ** 2 / (2.0 * sigma * sigma))
        key = jax.random.key(seed)
        k_z, k_d, k_w = jax.random.split(key, 3)
        z = jax.random.normal(k_z, (N, D), dtype=jnp.float32)
        dist_matrix = jax.random.uniform(k_d, (N, N), dtype=jnp.float32) * 2.0 + 0.05
        W = jax.random.normal(k_w, (D, D), dtype=jnp.float32)
        B = jnp.zeros((D,), dtype=jnp.float32)
        return {'z': z, 'dist_matrix': dist_matrix, 'W': W, 'B': B}
    _L1_gnn_all = _L1_gnn_setup()
    _L1_gnn_in = {k: v for k, v in _L1_gnn_all.items() if k in ('W', 'B')}
    del _L1_gnn_all
    return {'x': x, 'adj': adj, 'L0_gnn_W': _L0_gnn_in['W'], 'L0_gnn_a': _L0_gnn_in['a'], 'L1_gnn_W': _L1_gnn_in['W'], 'L1_gnn_B': _L1_gnn_in['B']}

def reference(x, adj, L0_gnn_W, L0_gnn_a, L1_gnn_W, L1_gnn_B):
    import jax
    import jax.numpy as jnp

    def _L0_gnn_ref(x, adj, W, a):
        import jax, jax.numpy as jnp
        import numpy as np
        NEG_INF = -9000000000000000.0
        NEG_SLOPE = 0.2
        d_out = W.shape[1]
        Wh = x @ W
        e_src = Wh @ a[:d_out]
        e_dst = Wh @ a[d_out:]
        e = jax.nn.leaky_relu(e_src[:, None] + e_dst[None, :], NEG_SLOPE)
        N = Wh.shape[0]
        mask = (adj > 0) | jnp.eye(N, dtype=bool)
        e = jnp.where(mask, e, NEG_INF)
        alpha = jax.nn.softmax(e, axis=1)
        h = alpha @ Wh
        return h

    def _L1_gnn_ref(z, dist_matrix, W, B):
        import jax, jax.numpy as jnp
        import numpy as np
        N = 4096
        D = 128
        CUTOFF = 1.0
        MU = 1.0
        SIGMA = 0.5

        def sensitivity(r, mu, sigma):
            return jnp.exp(-(1.0 / r - 1.0 / mu) ** 2 / (2.0 * sigma * sigma))
        msg = z @ W + B
        sens = sensitivity(dist_matrix, MU, SIGMA)
        weights = jnp.where(dist_matrix < CUTOFF, sens, 0.0)
        return weights @ msg
    h = jnp.maximum(_layernorm(x, axis=-1), 0.0)
    x = x + _L0_gnn_ref(h, adj, L0_gnn_W, L0_gnn_a)
    h = jnp.maximum(_layernorm(x, axis=-1), 0.0)
    x = x + _L1_gnn_ref(h, adj, L1_gnn_W, L1_gnn_B)
    return x

_drawn_inputs = setup_inputs


def setup_inputs(seed=0):
    import zlib

    import numpy as np

    out = dict(_drawn_inputs(seed))
    spreads = {'L1_gnn_B': (0.0, 0.1)}
    factors = {}
    for name, (base, spread) in spreads.items():
        noise = np.random.default_rng([zlib.crc32(name.encode()), seed]).standard_normal(out[name].shape)
        drawn = base * np.exp(spread * noise) if base else spread * noise
        out[name] = jnp.asarray(drawn.astype(out[name].dtype))
    for name, factor in factors.items():
        out[name] = (out[name] * factor).astype(out[name].dtype)
    return out
```

```python
import concourse.bass as bass
from concourse import mybir
from contextlib import ExitStack

REDUCE_MAX = bass.bass_isa.ReduceOp.max
N, D, P = 4096, 128, 128
NB = N // P
ST = 512
NS = N // ST
KB = ST // P
CW = 1024
NCH = N // CW
GW = 2
GPC = CW // (GW * P)
GPS = NCH * GPC
E1 = D + 1
E2 = D + 2
XQ = 4
BPQ = NB // XQ
TB = 4
WR = 4
MR = 2
G0_STEPS = 18
G1_STEPS = 4
RECIPROCAL_MAX = 1.0e18
EPS = 1e-5
SLOPE = 0.2
RANGE = 20.0
MASKED = -3.0e38
BELOW_ONE = 1.0 - 2.0 ** -24
STEEP = 2.0 ** 100


def gnn_program(nc, x, adj, w0, a0, w1, b1, out):
    fp32, bf16, i32 = mybir.dt.float32, mybir.dt.bfloat16, mybir.dt.int32
    ALU, ACT, AX = mybir.AluOpType, mybir.ActivationFunctionType, mybir.AxisListType

    adj_chunks = adj.rearrange("(s k p) (c n) -> s c p k n", k=KB, p=P, n=CW)
    adj_tiles = adj.rearrange("(t p) n -> t p n", p=P)
    x_quarters = x.rearrange("(q b p) d -> q p b d", q=XQ, p=P)
    out_super = out.rearrange("(s k p) d -> s p k d", k=KB, p=P)
    out_tiles = out.rearrange("(t p) d -> t p d", p=P)
    adj_diagonal = bass.AP(adj.tensor, adj.offset, [[N + 1, P], [(N + 1) * P, NB]])

    ctx = ExitStack()
    with ctx:
        def sb(name, shape, dt=fp32):
            return ctx.enter_context(nc.sbuf_tensor(name, shape, dt))

        def sem(name):
            return ctx.enter_context(nc.semaphore(name))

        ring = sb("adj_ring", [P, NCH, KB * CW])
        x_sb = sb("x_sb", [P, NB, D])
        hT = sb("hT", [P, N])
        whe = sb("whe", [P, NB, E2])
        aw = sb("aw", [P, NB, E1])
        row = sb("row", [P, N])
        scratch = sb("scratch", [P, WR + MR, GW * ST])
        weights = scratch[:, 0:WR, :]
        unmasked = scratch[:, WR:WR + MR, :]
        unread = sb("unread", [P, 2, KB * CW], bf16)
        x1_out = sb("x1_out", [P, 2, KB, D])
        summed = sb("summed", [P, KB, E1])
        rden = sb("rden", [P, KB])
        ident = sb("ident", [P, P])
        ident_h = sb("ident_h", [P, P], bf16)
        offdiag = sb("offdiag", [P, P])
        w0_sb = sb("w0_sb", [P, E2])
        w0T = sb("w0T", [P, D])
        a_sb = sb("a_sb", [P, 2])
        src_cols = sb("src_cols", [P, P])
        dst_cols = sb("dst_cols", [P, P])
        ones = sb("ones", [P, P])
        stats = sb("stats", [P, NB, 6])
        mv = sb("mv", [P, NB, 2])
        std = sb("std", [P, NB])
        rstd = sb("rstd", [P, NB])
        eps_t = sb("eps_t", [P, 1])
        below_one = sb("below_one", [P, 1])
        minus_one = sb("minus_one", [P, 1])
        q_col = sb("q_col", [P, NB])
        diag = sb("diag", [P, NB])
        sd_sum = sb("sd_sum", [P, NB])
        pair_ii = sb("pair_ii", [P, NB])
        w_self = sb("w_self", [P, NB])
        w_diag = sb("w_diag", [P, NB])
        ends = sb("ends", [P, 4])
        ends_all = sb("ends_all", [P, 4])
        neg_dmax = sb("neg_dmax", [P, 1])
        signs = sb("signs", [P, NS * NCH])
        zeros = sb("zeros", [P, NS * NCH])
        balance = sb("balance", [P, NS * NCH])
        plain = sb("plain", [P, NS * NCH])
        plain_all = sb("plain_all", [P, 1])
        end_max = sb("end_max", [P, 1])
        good = sb("good", [P, 1])
        bad = sb("bad", [P, 1])
        bad_all = sb("bad_all", [P, 1])
        flag = sb("flag", [P, 1], i32)
        w1_sb = sb("w1_sb", [P, D])
        b1_sb = sb("b1_sb", [P, D])
        s_tile = sb("s_tile", [P, 1])
        top = sb("top", [P, 1])
        top_s = sb("top_s", [P, 1])
        top_l = sb("top_l", [P, 1])
        neg_top = sb("neg_top", [P, 1])
        den = sb("den", [P, 1])
        x1_tile = sb("x1_tile", [P, D])
        h2 = sb("h2", [P, D])
        h2T = sb("h2T", [P, D])

        ring_h = ring[:, :, :].bitcast(bf16).rearrange("p c (k n two) -> p c k n two", k=KB, two=2)
        g_adj, g_score, g_weight, g_wT = (ring[:, n, :] for n in range(4))
        msg = aw[:, :, 0:D]

        def hn_block(b):
            return scratch[:, b // BPQ, (b % BPQ) * P:(b % BPQ + 1) * P]

        diag_h = diag[:, :].bitcast(bf16).rearrange("p (b two) -> p b two", two=2)

        bank = [ctx.enter_context(nc.psum_tensor(f"bank{n}", [P, 512], fp32)) for n in range(8)]
        tr_bank = [bank[n][:, :].bitcast(bf16) for n in range(TB)]
        acc = [[bank[4 + 2 * par + half] for half in range(2)] for par in range(2)]

        def acc_of(par, k):
            return acc[par][k // 2][:, (k % 2) * E1:(k % 2 + 1) * E1]

        w_loaded, a_loaded, diag_loaded = sem("w_loaded"), sem("a_loaded"), sem("diag_loaded")
        x_loaded = [sem(f"x_loaded{q}") for q in range(XQ)]
        adj_ready = [sem(f"adj_ready{c}") for c in range(NCH)]
        consts_set, ident_set = sem("consts_set"), sem("ident_set")
        w0T_done, w0T_copied, wa_done, wa_copied, cols_set = (
            sem(n) for n in ("w0T_done", "w0T_copied", "wa_done", "wa_copied", "cols_set"))
        ln_step, std_done, hn_done, hT_done, hT_copied = (
            sem(n) for n in ("ln_step", "std_done", "hn_done", "hT_done", "hT_copied"))
        whe_done, whe_copied, srow_done, row_set = (
            sem(n) for n in ("whe_done", "whe_copied", "srow_done", "row_set"))
        ends_step, ends_reduced, dmax_set, a_set, q_set, aw_set, sd_set, pair_done, self_step = (
            sem(n) for n in ("ends_step", "ends_reduced", "dmax_set", "a_set", "q_set", "aw_set", "sd_set",
                             "pair_done", "self_step"))
        stats_set, rstd_set, end_max_set = sem("stats_set"), sem("rstd_set"), sem("end_max_set")
        transposed, unmasked_set, masked, mm_done, signs_taken, checked = (
            sem(n) for n in ("transposed", "unmasked_set", "masked", "mm_done", "signs_taken", "checked"))
        finish_step, finished, stored = sem("finish_step"), sem("finished"), sem("stored")
        verdict_step, bad_reduced, flag_set = sem("verdict_step"), sem("bad_reduced"), sem("flag_set")
        g_w1, g_b1, g_loaded, g_drow, g_drow_set = (
            sem(n) for n in ("g_w1", "g_b1", "g_loaded", "g_drow", "g_drow_set"))
        g0_vec, g0_exp, g0_tr, g0_ev, g0_mm, g0_std, g0_h2tr, g0_h2T, g0_msg = (
            sem(n) for n in ("g0_vec", "g0_exp", "g0_tr", "g0_ev", "g0_mm", "g0_std", "g0_h2tr",
                             "g0_h2T", "g0_msg"))
        g1_loaded, g1_vec, g1_act, g1_tr, g1_ev, g1_mm, g1_stored = (
            sem(n) for n in ("g1_loaded", "g1_vec", "g1_act", "g1_tr", "g1_ev", "g1_mm", "g1_stored"))

        block = ctx.enter_context(nc.Block())

        @block.sync
        def _(sp):
            sp.dma_start(w0_sb[:, 0:D], w0).then_inc(w_loaded, 16)
            with nc.allow_non_contiguous_dma(reason="256 values"):
                sp.dma_start(a_sb[:, :], a0.rearrange("(c d) -> d c", c=2)).then_inc(a_loaded, 16)
            for q in range(XQ):
                sp.dma_start(x_sb[:, q * BPQ:(q + 1) * BPQ, :], x_quarters[q]).then_inc(x_loaded[q], 16)

            def load_chunk(s, c):
                sp.dma_start(ring[:, c, :].rearrange("p (k n) -> p k n", k=KB),
                             adj_chunks[s, c]).then_inc(adj_ready[c], 16)

            def load_into_used_slot(s, c):
                sp.wait_ge(transposed, ((s - 1) * NCH + c + 1) * GPC)
                sp.wait_ge(checked, (s - 1) * NCH + c + 1)
                load_chunk(s, c)

            def store(s, par):
                sp.wait_ge(finished, s + 1)
                sp.dma_start(out_super[s], x1_out[:, par]).then_inc(stored, 16)

            load_chunk(0, 0)
            with nc.allow_non_contiguous_dma(reason="4096 values"):
                sp.dma_start(diag[:, :], adj_diagonal).then_inc(diag_loaded, 16)
            for c in range(1, NCH):
                load_chunk(0, c)
            for c in range(NCH):
                load_into_used_slot(1, c)
            with sp.Fori(1, NS // 2) as it:
                for par in range(2):
                    s = it * 2 + par
                    load_into_used_slot(s, 0)
                    load_into_used_slot(s, 1)
                    store(s - 2, par)
                    load_into_used_slot(s, 2)
                    load_into_used_slot(s, 3)
            store(NS - 2, 0)
            store(NS - 1, 1)
            sp.wait_ge(stored, 16 * NS)

            sp.wait_ge(flag_set, 1)
            general = sp.value_load(flag[0:1, 0:1])
            with sp.If(general != 0):
                sp.dma_start(w1_sb[:, :], w1).then_inc(g_w1, 16)
                sp.dma_start(b1_sb[:, :], b1.partition_broadcast(P)).then_inc(g_b1, 16)
                sp.dma_start(g_adj, adj_tiles[0]).then_inc(g_loaded, 16)
                with sp.Fori(1, NB) as t:
                    sp.wait_ge(g0_vec, G0_STEPS * (t - 1) + 1)
                    sp.dma_start(g_adj, adj_tiles[t]).then_inc(g_loaded, 16)
                sp.wait_ge(g0_vec, G0_STEPS * (NB - 1) + 1)
                sp.dma_start(g_adj, adj_tiles[0]).then_inc(g1_loaded, 16)
                with sp.Fori(0, NB - 1) as t:
                    sp.wait_ge(g1_vec, G1_STEPS * t + G1_STEPS)
                    sp.dma_start(out_tiles[t], x1_out[:, 0, 0, :]).then_inc(g1_stored, 16)
                    sp.dma_start(g_adj, adj_tiles[t + 1]).then_inc(g1_loaded, 16)
                sp.wait_ge(g1_vec, G1_STEPS * NB)
                sp.dma_start(out_tiles[NB - 1], x1_out[:, 0, 0, :]).then_inc(g1_stored, 16)
                sp.wait_ge(g1_stored, 16 * NB)

        @block.gpsimd
        def _(pool):
            nc.gpsimd.memset(ident[:, :], 0.0).then_inc(consts_set, 1)
            nc.gpsimd.memset(ident_h[:, :], 0.0).then_inc(consts_set, 1)
            nc.gpsimd.memset(offdiag[:, :], 1.0).then_inc(consts_set, 1)
            nc.gpsimd.memset(ones[:, :], 1.0).then_inc(consts_set, 1)
            nc.gpsimd.memset(eps_t[:, :], EPS).then_inc(consts_set, 1)
            nc.gpsimd.memset(below_one[:, :], BELOW_ONE).then_inc(consts_set, 1)
            nc.gpsimd.memset(minus_one[:, :], -1.0).then_inc(consts_set, 1)
            pool.wait_ge(consts_set, 7)
            for tile, fill in ((ident, 1.0), (ident_h, 1.0), (offdiag, 0.0)):
                nc.gpsimd.affine_select(out=tile[:, :], in_=tile[:, :], compare_op=ALU.not_equal, fill=fill,
                                        base=0, pattern=[[-1, P]], channel_multiplier=1).then_inc(ident_set, 1)
            pool.wait_ge(ends_step, 4)
            nc.gpsimd.partition_all_reduce(ends_all[:, :], ends[:, :], P,
                                           REDUCE_MAX).then_inc(ends_reduced, 1)
            pool.wait_ge(verdict_step, 5)
            nc.gpsimd.partition_all_reduce(bad_all[:, :], bad[:, :], P,
                                           REDUCE_MAX).then_inc(bad_reduced, 1)

        @block.tensor
        def _(pe):
            pe.wait_ge(ident_set, 3)
            pe.wait_ge(w_loaded, 16)
            nc.tensor.transpose(bank[7][:, 0:D], w0_sb[:, 0:D], ident[:, :]).then_inc(w0T_done, 1)
            pe.wait_ge(w0T_copied, 1)
            pe.wait_ge(a_loaded, 16)
            nc.tensor.matmul(bank[6][:, 0:2], w0T[:, :], a_sb[:, :], start=True, stop=True).then_inc(wa_done, 1)

            def transpose_h(n):
                pe.wait_ge(hn_done, n + 1)
                if n >= 2:
                    pe.wait_ge(hT_copied, n - 1)
                for b in range(4):
                    last = nc.tensor.transpose(bank[n % 2][:, b * P:(b + 1) * P],
                                               hn_block(4 * n + b), ident[:, :])
                last.then_inc(hT_done, 1)

            def project(n):
                pe.wait_ge(hT_copied, n + 1)
                for half in range(2):
                    m = 2 * n + half
                    if m >= 2:
                        pe.wait_ge(whe_copied, m - 1)
                    for b in range(2):
                        nb = 2 * m + b
                        last = nc.tensor.matmul(bank[2 + m % 2][:, b * E2:(b + 1) * E2], hT[:, nb * P:(nb + 1) * P],
                                                w0_sb[:, :], start=(b == 0), stop=(b == 1), skip_group_check=True)
                    last.then_inc(whe_done, 1)
                if n >= 2:
                    pe.wait_ge(row_set, n - 1)
                nc.tensor.matmul(bank[4 + n % 2][:, :], src_cols[:, :], hT[:, n * 512:(n + 1) * 512],
                                 start=True, stop=True).then_inc(srow_done, 1)

            transpose_h(0)
            pe.wait_ge(wa_copied, 1)
            pe.wait_ge(cols_set, 2)
            for n in range(NB // 4):
                if n + 1 < NB // 4:
                    transpose_h(n + 1)
                project(n)
            pe.wait_ge(hT_copied, NB // 4)
            pe.wait_ge(whe_copied, NB // 2)
            pe.wait_ge(row_set, NB // 4)

            def transpose_group(it, gg, first):
                par, g = gg // GPS, gg % GPS
                c, part = g // GPC, g % GPC
                q = it * (2 * GPS) + gg
                if part == 0:
                    pe.wait_ge(adj_ready[c], (it * 2 + par + 1) * 16)
                if not first or gg >= TB:
                    pe.wait_ge(masked, q - TB + 1)
                for b in range(GW):
                    col = (part * GW + b) * P
                    for k in range(KB):
                        last = nc.tensor.transpose(tr_bank[gg % TB][:, b * ST + k * P:b * ST + (k + 1) * P],
                                                   ring_h[:, c, k, col:col + P, 1], ident_h[:, :])
                last.then_inc(transposed, 1)

            def multiply_group(it, gg, first, wslot):
                par, g = gg // GPS, gg % GPS
                q = it * (2 * GPS) + gg
                if g == 0 and not first:
                    pe.wait_ge(finished, it * 2 + par - 1)
                pe.wait_ge(masked, q + 1)
                for b in range(GW):
                    jb = GW * g + b
                    if first and par == 0 and jb % BPQ == 0:
                        pe.wait_ge(aw_set, jb // BPQ + 1)
                    for k in range(KB):
                        last = nc.tensor.matmul(acc_of(par, k), weights[:, wslot, b * ST + k * P:b * ST + (k + 1) * P],
                                                aw[:, jb, :], start=(jb == 0 and k % 2 == 0), stop=(jb == NB - 1),
                                                skip_group_check=True)
                last.then_inc(mm_done, 1)

            def pair_of_supertiles(it, first, last):
                for gg in range(2 * GPS):
                    if gg + 2 < 2 * GPS:
                        transpose_group(it, gg + 2, first)
                    elif not last:
                        transpose_group(it + 1, gg + 2 - 2 * GPS, False)
                    multiply_group(it, gg, first, gg % WR)

            transpose_group(0, 0, True)
            transpose_group(0, 1, True)
            pair_of_supertiles(0, True, False)
            with pe.Fori(1, NS // 2 - 1) as it:
                pair_of_supertiles(it, False, False)
            pair_of_supertiles(NS // 2 - 1, False, True)

            def general_transposes(tr, ev, t):
                for n in range(8):
                    if n >= 4:
                        pe.wait_ge(ev, t * 8 + n - 3)
                    for b in range(4):
                        jb = 4 * n + b
                        last = nc.tensor.transpose(bank[n % 4][:, b * P:(b + 1) * P],
                                                   g_weight[:, jb * P:(jb + 1) * P], ident[:, :])
                    last.then_inc(tr, 1)

            pe.wait_ge(flag_set, 1)
            general = pe.value_load(flag[0:1, 0:1])
            with pe.If(general != 0):
                for n in range(8):
                    if n >= 2:
                        pe.wait_ge(g_drow_set, n - 1)
                    nc.tensor.matmul(bank[n % 2][:, :], dst_cols[:, :], hT[:, n * 512:(n + 1) * 512],
                                     start=True, stop=True).then_inc(g_drow, 1)
                pe.wait_ge(g_drow_set, 8)
                pe.wait_ge(g_w1, 16)
                with pe.Fori(0, NB) as t:
                    pe.wait_ge(g0_exp, t + 1)
                    general_transposes(g0_tr, g0_ev, t)
                    pe.wait_ge(g0_ev, t * 8 + 8)
                    for jb in range(NB):
                        last = nc.tensor.matmul(bank[4][:, 0:D], g_wT[:, jb * P:(jb + 1) * P], whe[:, jb, 0:D],
                                                start=(jb == 0), stop=(jb == NB - 1))
                    last.then_inc(g0_mm, 1)
                    pe.wait_ge(g0_vec, G0_STEPS * t + G0_STEPS - 1)
                    nc.tensor.transpose(bank[5][:, 0:P], h2[:, :], ident[:, :]).then_inc(g0_h2tr, 1)
                    pe.wait_ge(g0_h2T, t + 1)
                    nc.tensor.matmul(bank[6][:, 0:D], h2T[:, :], w1_sb[:, :],
                                     start=True, stop=True).then_inc(g0_msg, 1)
                pe.wait_ge(g0_vec, G0_STEPS * NB)
                with pe.Fori(0, NB) as t:
                    pe.wait_ge(g1_vec, G1_STEPS * t + 3)
                    general_transposes(g1_tr, g1_ev, t)
                    pe.wait_ge(g1_ev, t * 8 + 8)
                    for jb in range(NB):
                        last = nc.tensor.matmul(bank[4][:, 0:D], g_wT[:, jb * P:(jb + 1) * P], msg[:, jb, :],
                                                start=(jb == 0), stop=(jb == NB - 1))
                    last.then_inc(g1_mm, 1)

        @block.scalar
        def _(act):
            act.wait_ge(consts_set, 7)
            for q in range(XQ):
                act.wait_ge(ln_step, q + 1)
                nc.scalar.activation(std[:, q * BPQ:(q + 1) * BPQ], mv[:, q * BPQ:(q + 1) * BPQ, 1],
                                     ACT.Sqrt, bias=eps_t[:, :]).then_inc(std_done, 1)

            def rectify(n):
                act.wait_ge(hT_done, n + 1)
                nc.scalar.activation(hT[:, n * 512:(n + 1) * 512], bank[n % 2][:, :],
                                     ACT.Relu).then_inc(hT_copied, 1)

            def r_row(n):
                act.wait_ge(srow_done, n + 1)
                nc.scalar.activation(row[:, n * 512:(n + 1) * 512], bank[4 + n % 2][:, :], ACT.Exp,
                                     scale=-(1 - SLOPE)).then_inc(row_set, 1)

            rectify(0)
            for n in range(NB // 4):
                if n + 1 < NB // 4:
                    rectify(n + 1)
                r_row(n)
            act.wait_ge(whe_copied, NB // 2)
            nc.scalar.activation(q_col[:, :], whe[:, :, D + 1], ACT.Exp, scale=-(1 - SLOPE)).then_inc(q_set, 1)
            act.wait_ge(dmax_set, 1)
            nc.scalar.activation(aw[:, :, D], whe[:, :, D + 1], ACT.Exp, bias=neg_dmax[:, :]).then_inc(a_set, 1)
            act.wait_ge(sd_set, 1)
            nc.scalar.activation(pair_ii[:, :], sd_sum[:, :], ACT.Exp, scale=-(1 - SLOPE)).then_inc(pair_done, 1)

            def count_entries(s, c, first):
                n = s * NCH + c
                act.wait_ge(adj_ready[c], (s + 1) * 16)
                if not first:
                    act.wait_ge(signs_taken, n)
                nc.scalar.activation(unread[:, 0], ring[:, c, :], ACT.Sign, bias=below_one[:, :], scale=-1.0,
                                     accum_out=signs[:, bass.ds(n, 1)]).then_inc(signs_taken, 1)
                if not first:
                    act.wait_ge(checked, n)
                nc.scalar.activation(unread[:, 1], ring[:, c, :], ACT.Exp, scale=-STEEP,
                                     accum_out=zeros[:, bass.ds(n, 1)]).then_inc(checked, 1)

            for c in range(NCH):
                count_entries(0, c, c == 0)
            with act.Fori(1, NS) as s:
                for c in range(NCH):
                    count_entries(s, c, False)

            def general_copies(tr, ev, t):
                for n in range(8):
                    act.wait_ge(tr, t * 8 + n + 1)
                    nc.scalar.activation(g_wT[:, n * 512:(n + 1) * 512], bank[n % 4][:, :],
                                         ACT.Copy).then_inc(ev, 1)

            act.wait_ge(flag_set, 1)
            general = act.value_load(flag[0:1, 0:1])
            with act.If(general != 0):
                for n in range(8):
                    act.wait_ge(g_drow, n + 1)
                    nc.scalar.activation(row[:, n * 512:(n + 1) * 512], bank[n % 2][:, :],
                                         ACT.Copy).then_inc(g_drow_set, 1)
                with act.Fori(0, NB) as t:
                    act.wait_ge(g0_vec, G0_STEPS * t + 10)
                    nc.scalar.activation(g_weight, g_score, ACT.Exp, bias=neg_top[:, :],
                                         accum_out=den[:, :]).then_inc(g0_exp, 1)
                    general_copies(g0_tr, g0_ev, t)
                    act.wait_ge(g0_vec, G0_STEPS * t + 15)
                    nc.scalar.activation(std[:, 0:1], mv[:, 0, 1:2], ACT.Sqrt,
                                         bias=eps_t[:, :]).then_inc(g0_std, 1)
                    act.wait_ge(g0_h2tr, t + 1)
                    nc.scalar.activation(h2T[:, :], bank[5][:, 0:P], ACT.Relu).then_inc(g0_h2T, 1)
                with act.Fori(0, NB) as t:
                    act.wait_ge(g1_vec, G1_STEPS * t + 2)
                    nc.scalar.activation(g_weight, g_score, ACT.Square, bias=minus_one[:, :]).then_inc(g1_act, 1)
                    act.wait_ge(g1_act, t * 2 + 1)
                    nc.scalar.activation(g_score, g_weight, ACT.Exp, scale=-2.0).then_inc(g1_act, 1)
                    general_copies(g1_tr, g1_ev, t)

        @block.vector
        def _(dve):
            dve.wait_ge(consts_set, 7)
            dve.wait_ge(w0T_done, 1)
            nc.vector.tensor_copy(w0T[:, :], bank[7][:, 0:D]).then_inc(w0T_copied, 1)

            def layer_norm_quarter(q):
                dve.wait_ge(x_loaded[q], 16)
                for b in range(q * BPQ, (q + 1) * BPQ):
                    last = nc.vector.bn_stats(stats[:, b, :], x_sb[:, b, :])
                last.then_inc(stats_set, 1)
                dve.wait_ge(stats_set, q + 1)
                for b in range(q * BPQ, (q + 1) * BPQ):
                    last = nc.vector.bn_aggr(mv[:, b, :], stats[:, b, :])
                last.then_inc(ln_step, 1)

            def normalise_quarter(q):
                quarter = slice(q * BPQ, (q + 1) * BPQ)
                dve.wait_ge(std_done, q + 1)
                nc.vector.reciprocal(rstd[:, quarter], std[:, quarter]).then_inc(rstd_set, 1)
                dve.wait_ge(rstd_set, q + 1)
                for half in range(2):
                    for b in range(q * BPQ + 4 * half, q * BPQ + 4 * half + 4):
                        last = nc.vector.tensor_scalar(hn_block(b), x_sb[:, b, :], mv[:, b, 0:1], rstd[:, b:b + 1],
                                                       ALU.subtract, ALU.mult)
                    last.then_inc(hn_done, 1)

            layer_norm_quarter(0)
            dve.wait_ge(wa_done, 1)
            nc.vector.tensor_copy(w0_sb[:, D:D + 2], bank[6][:, 0:2]).then_inc(wa_copied, 1)
            nc.vector.tensor_scalar(src_cols[:, :], ones[:, :], bank[6][:, 0:1], None, ALU.mult).then_inc(cols_set, 1)
            nc.vector.tensor_scalar(dst_cols[:, :], ones[:, :], bank[6][:, 1:2], None, ALU.mult).then_inc(cols_set, 1)
            layer_norm_quarter(1)
            normalise_quarter(0)
            layer_norm_quarter(2)
            normalise_quarter(1)
            layer_norm_quarter(3)
            normalise_quarter(2)
            normalise_quarter(3)
            for m in range(NB // 2):
                dve.wait_ge(whe_done, m + 1)
                nc.vector.tensor_copy(whe[:, 2 * m:2 * m + 2, :],
                                      bank[2 + m % 2][:, 0:2 * E2].rearrange("p (b n) -> p b n", b=2)).then_inc(whe_copied, 1)
            dve.wait_ge(whe_copied, NB // 2)
            for n, (col, op, neg) in enumerate(((D + 1, ALU.max, False), (D + 1, ALU.min, True),
                                                (D, ALU.max, False), (D, ALU.min, True))):
                nc.vector.tensor_reduce(ends[:, n:n + 1], whe[:, :, col], AX.X, op, negate=neg).then_inc(ends_step, 1)
            nc.vector.tensor_tensor(sd_sum[:, :], whe[:, :, D], whe[:, :, D + 1], ALU.add).then_inc(sd_set, 1)
            dve.wait_ge(ends_reduced, 1)
            nc.vector.tensor_scalar(neg_dmax[:, :], ends_all[:, 0:1], -1.0, None, ALU.mult).then_inc(dmax_set, 1)
            nc.vector.tensor_reduce(end_max[:, :], ends_all[:, :], AX.X, ALU.max).then_inc(end_max_set, 1)

            def weigh_features(q):
                quarter = slice(q * BPQ, (q + 1) * BPQ)
                nc.vector.tensor_tensor(aw[:, quarter, 0:D], whe[:, quarter, 0:D],
                                        aw[:, quarter, D:D + 1].broadcast_to([P, BPQ, D]), ALU.mult).then_inc(aw_set, 1)

            def self_edges():
                dve.wait_ge(pair_done, 1)
                nc.vector.tensor_scalar(w_self[:, :], pair_ii[:, :], 1.0, None, ALU.max).then_inc(self_step, 1)
                dve.wait_ge(self_step, 1)
                dve.wait_ge(diag_loaded, 16)
                nc.vector.scalar_tensor_tensor(w_diag[:, :], diag_h[:, :, 1], 0.0, w_self[:, :],
                                               ALU.is_le, ALU.mult).then_inc(self_step, 1)
                dve.wait_ge(self_step, 2)

            def unmask_group(it, gg, first):
                par, g = gg // GPS, gg % GPS
                q = it * (2 * GPS) + gg
                if not first or gg >= MR:
                    dve.wait_ge(masked, q - MR + 1)
                for b in range(GW):
                    jb = GW * g + b
                    last = nc.vector.tensor_scalar(unmasked[:, gg % MR, b * ST:(b + 1) * ST],
                                                   row[:, bass.ds((it * 2 + par) * ST, ST)],
                                                   q_col[:, jb:jb + 1], 1.0, ALU.mult, ALU.max)
                last.then_inc(unmasked_set, 1)

            def mask_group(it, gg, first):
                q = it * (2 * GPS) + gg
                dve.wait_ge(transposed, q + 1)
                dve.wait_ge(unmasked_set, q + 1)
                if not first or gg >= WR:
                    dve.wait_ge(mm_done, q - WR + 1)
                nc.vector.scalar_tensor_tensor(weights[:, gg % WR, :], tr_bank[gg % TB], 0.0,
                                               unmasked[:, gg % MR, :], ALU.is_gt, ALU.mult).then_inc(masked, 1)

            def finish_supertile(it, par, first):
                s = it * 2 + par
                dve.wait_ge(mm_done, (s + 1) * GPS)
                for k in range(KB):
                    last = nc.vector.scalar_tensor_tensor(summed[:, k, :], aw[:, bass.ds(s * KB + k, 1), :],
                                                          w_diag[:, bass.ds(s * KB + k, 1)], acc_of(par, k),
                                                          ALU.mult, ALU.add)
                last.then_inc(finish_step, 1)
                dve.wait_ge(finish_step, s * 2 + 1)
                nc.vector.reciprocal(rden[:, :], summed[:, :, D]).then_inc(finish_step, 1)
                dve.wait_ge(finish_step, s * 2 + 2)
                if not first:
                    dve.wait_ge(stored, (s - 1) * 16)
                for k in range(KB):
                    last = nc.vector.scalar_tensor_tensor(x1_out[:, par, k, :], summed[:, k, 0:D], rden[:, k:k + 1],
                                                          x_sb[:, bass.ds(s * KB + k, 1), :], ALU.mult, ALU.add)
                last.then_inc(finished, 1)

            def pair_of_supertiles(it, first, last):
                for gg in range(2 * GPS):
                    if gg + 1 < 2 * GPS:
                        unmask_group(it, gg + 1, first)
                    elif not last:
                        unmask_group(it + 1, 0, False)
                    mask_group(it, gg, first)
                    if first and gg + 1 < XQ:
                        weigh_features(gg + 1)
                    if first and gg == XQ:
                        self_edges()
                    if gg == GPS + 3:
                        finish_supertile(it, 0, first)
                    elif gg == 3 and not first:
                        finish_supertile(it - 1, 1, first=False)
                if last:
                    finish_supertile(it, 1, first=False)

            dve.wait_ge(a_set, 1)
            weigh_features(0)
            dve.wait_ge(q_set, 1)
            dve.wait_ge(row_set, NB // 4)
            dve.wait_ge(hT_done, NB // 4)
            unmask_group(0, 0, True)
            pair_of_supertiles(0, True, False)
            with dve.Fori(1, NS // 2 - 1) as it:
                pair_of_supertiles(it, False, False)
            pair_of_supertiles(NS // 2 - 1, False, True)

            def verdict(ins, n):
                ins.then_inc(verdict_step, 1)
                dve.wait_ge(verdict_step, n)

            dve.wait_ge(checked, NS * NCH)
            verdict(nc.vector.scalar_tensor_tensor(balance[:, :], zeros[:, :], -2.0, signs[:, :],
                                                   ALU.mult, ALU.add), 1)
            verdict(nc.vector.tensor_scalar(plain[:, :], balance[:, :], -float(KB * CW), None, ALU.is_equal), 2)
            verdict(nc.vector.tensor_reduce(plain_all[:, :], plain[:, :], AX.X, ALU.min), 3)
            dve.wait_ge(end_max_set, 1)
            verdict(nc.vector.tensor_scalar(good[:, :], end_max[:, :], RANGE, plain_all[:, :], ALU.is_le, ALU.mult), 4)
            verdict(nc.vector.tensor_scalar(bad[:, :], good[:, :], -1.0, 1.0, ALU.mult, ALU.add), 5)
            dve.wait_ge(bad_reduced, 1)
            nc.vector.tensor_copy(flag[:, :], bad_all[:, :]).then_inc(flag_set, 1)

            dve.wait_ge(flag_set, 1)
            general = dve.value_load(flag[0:1, 0:1])
            with dve.If(general != 0):
                dve.wait_ge(g_drow_set, 8)
                dve.wait_ge(g_b1, 16)
                with dve.Fori(0, NB) as t:
                    def step(ins, n):
                        ins.then_inc(g0_vec, 1)
                        dve.wait_ge(g0_vec, G0_STEPS * t + n)

                    dve.wait_ge(g_loaded, t * 16 + 16)
                    step(nc.vector.tensor_scalar(g_score, g_adj, 0.0, MASKED, ALU.is_le, ALU.mult), 1)
                    own = g_score[:, bass.ds(t * P, P)]
                    step(nc.vector.tensor_tensor(own, own, offdiag[:, :], ALU.mult), 2)
                    step(nc.vector.tensor_tensor(g_score, g_score, row[:, :], ALU.add), 3)
                    step(nc.vector.tensor_scalar(s_tile[:, :], whe[:, bass.ds(t, 1), D], 1.0, None, ALU.mult), 4)
                    step(nc.vector.tensor_reduce(top[:, :], g_score, AX.X, ALU.max), 5)
                    step(nc.vector.tensor_scalar(g_score, g_score, s_tile[:, :], None, ALU.add), 6)
                    step(nc.vector.scalar_tensor_tensor(g_score, g_score, SLOPE, g_score, ALU.mult, ALU.max), 7)
                    step(nc.vector.tensor_tensor(top_s[:, :], top[:, :], s_tile[:, :], ALU.add), 8)
                    step(nc.vector.scalar_tensor_tensor(top_l[:, :], top_s[:, :], SLOPE, top_s[:, :],
                                                        ALU.mult, ALU.max), 9)
                    step(nc.vector.tensor_scalar(neg_top[:, :], top_l[:, :], -1.0, None, ALU.mult), 10)
                    dve.wait_ge(g0_exp, t + 1)
                    step(nc.vector.reciprocal(rden[:, 0:1], den[:, :]), 11)
                    dve.wait_ge(g0_mm, t + 1)
                    step(nc.vector.scalar_tensor_tensor(x1_tile[:, :], bank[4][:, 0:D], rden[:, 0:1],
                                                        x_sb[:, bass.ds(t, 1), :], ALU.mult, ALU.add), 12)
                    step(nc.vector.bn_stats(stats[:, 0, :], x1_tile[:, :]), 13)
                    nc.vector.tensor_scalar(x_sb[:, bass.ds(t, 1), :], x1_tile[:, :], 1.0, None, ALU.mult).then_inc(g0_vec, 1)
                    step(nc.vector.bn_aggr(mv[:, 0, :], stats[:, 0, :]), 15)
                    dve.wait_ge(g0_std, t + 1)
                    step(nc.vector.reciprocal(rstd[:, 0:1], std[:, 0:1]), 16)
                    step(nc.vector.tensor_scalar(h2[:, :], x1_tile[:, :], mv[:, 0, 0:1], rstd[:, 0:1],
                                                 ALU.subtract, ALU.mult), 17)
                    dve.wait_ge(g0_msg, t + 1)
                    step(nc.vector.tensor_tensor(msg[:, bass.ds(t, 1), :], bank[6][:, 0:D], b1_sb[:, :], ALU.add), 18)
                with dve.Fori(0, NB) as t:
                    def step(ins, n):
                        ins.then_inc(g1_vec, 1)
                        dve.wait_ge(g1_vec, G1_STEPS * t + n)

                    dve.wait_ge(g1_loaded, t * 16 + 16)
                    step(nc.vector.reciprocal(g_score, g_adj), 1)
                    step(nc.vector.tensor_scalar(g_score, g_score, RECIPROCAL_MAX, -RECIPROCAL_MAX,
                                                 ALU.min, ALU.max), 2)
                    dve.wait_ge(g1_act, t * 2 + 2)
                    step(nc.vector.scalar_tensor_tensor(g_weight, g_adj, 1.0, g_score, ALU.is_lt, ALU.mult), 3)
                    dve.wait_ge(g1_mm, t + 1)
                    dve.wait_ge(g1_stored, t * 16)
                    step(nc.vector.tensor_tensor(x1_out[:, 0, 0, :], bank[4][:, 0:D], x_sb[:, bass.ds(t, 1), :],
                                                 ALU.add), 4)


_INS = ["x", "adj", "L0_gnn_W", "L0_gnn_a", "L1_gnn_W", "L1_gnn_B"]


def kernel(**inputs):
    import numpy as np
    import concourse.bacc as bacc
    from concourse.bass_utils import run_bass_kernel_spmd

    nc = bacc.Bacc("TRN2", target_bir_lowering=False, num_devices=1)
    arrays, args = {}, []
    for name in _INS:
        a = np.ascontiguousarray(inputs[name])
        arrays[f"in_{name}"] = a
        args.append(nc.dram_tensor(f"in_{name}", a.shape, mybir.dt.from_np(a.dtype), kind="ExternalInput").ap())
    args.append(nc.dram_tensor("out_0", (N, D), mybir.dt.float32, kind="ExternalOutput").ap())
    gnn_program(nc, *args)
    return run_bass_kernel_spmd(nc, [arrays], core_ids=[0]).results[0]["out_0"]
```

```python
import concourse.bass as bass
from concourse import mybir
from contextlib import ExitStack

REDUCE_MAX = bass.bass_isa.ReduceOp.max
N, D, P = 4096, 128, 128
NB = N // P
HR = 512
NH = N // HR
NS = NH // 2
KB = HR // P
CW = 1024
CPS = 2 * N // CW
AR = 4
GW = 4
GPS = N // (GW * P)
UPS = 2 * GPS
CR = 4
E1 = D + 1
E2 = D + 2
XO = 8
BPO = NB // XO
AQ = 4
BPQ = NB // AQ
MOMENTS_AHEAD = 3
TB = 4
WR = 2
MR = 2
POOL_STEPS = 12
G0_STEPS = 18
G1_STEPS = 6
RECIPROCAL_MAX = 1.0e18
TINY = 1.0e-30
EPS = 1e-5
SLOPE = 0.2
RANGE = 20.0
MASKED = -3.0e38
BELOW_ONE = 1.0 - 2.0 ** -24


def gnn_program(nc, x, adj, w0, a0, w1, b1, out):
    fp32, fp8, i32 = mybir.dt.float32, mybir.dt.float8e4, mybir.dt.int32
    ALU, ACT, AX = mybir.AluOpType, mybir.ActivationFunctionType, mybir.AxisListType

    adj_chunks = adj.rearrange("(s p k) (c n) -> s c p k n", k=KB, p=P, n=CW)
    adj_tiles = adj.rearrange("(s p k) n -> s k p n", p=P, k=KB)
    x_octants = x.rearrange("(o p k) d -> o p k d", p=P, k=KB)
    out_halves = out.rearrange("(s p k) d -> s p k d", k=KB, p=P)
    out_tiles = out.rearrange("(s p k) d -> s k p d", k=KB, p=P)
    adj_diagonal = [bass.AP(adj.tensor, adj.offset + k * (N + 1), [[KB * (N + 1), P], [HR * (N + 1), NH]])
                    for k in range(KB)]

    ctx = ExitStack()
    with ctx:
        def sb(name, shape, dt=fp32):
            return ctx.enter_context(nc.sbuf_tensor(name, shape, dt))

        def sem(name):
            return ctx.enter_context(nc.semaphore(name))

        ring = sb("adj_ring", [P, AR, KB * CW])
        x_sb = sb("x_sb", [P, NB, D])
        hT = sb("hT", [P, N])
        whe = sb("whe", [P, NB, E2])
        aw = sb("aw", [P, NB, E1])
        row = sb("row", [P, N])
        unmasked = sb("unmasked", [P, MR, GW, 2 * HR])
        weights = [hT[:, n * GW * HR:(n + 1) * GW * HR] for n in range(WR)]
        codes = sb("codes", [P, CR, KB * CW], fp8)
        summed = sb("summed", [P, 2, KB, E1])
        rden = sb("rden", [P, 2, KB])
        ident = sb("ident", [P, P])
        offdiag = sb("offdiag", [P, P])
        w0_sb = sb("w0_sb", [P, E2])
        w0T = sb("w0T", [P, D])
        a_sb = sb("a_sb", [P, 2])
        ones = sb("ones", [P, P])
        stats = sb("stats", [P, NB, 6])
        mv = sb("mv", [P, NB, 2])
        std = sb("std", [P, NB])
        rstd = sb("rstd", [P, NB])
        eps_t = sb("eps_t", [P, 1])
        below_one = sb("below_one", [P, 1])
        minus_one = sb("minus_one", [P, 1])
        q_col = sb("q_col", [P, NB])
        diag = sb("diag", [P, NB])
        sd_sum = sb("sd_sum", [P, NB])
        pair_ii = sb("pair_ii", [P, NB])
        w_self = sb("w_self", [P, NB])
        w_diag = sb("w_diag", [P, NB])
        ends = sb("ends", [P, 4])
        ends_all = sb("ends_all", [P, 4])
        neg_dmax = sb("neg_dmax", [P, 1])
        signs = sb("signs", [P, CPS])
        sizes = sb("sizes", [P, CPS])
        entries = sb("entries", [P, CPS // 2])
        excess = sb("excess", [P, 2, CPS // 2])
        excess_sum = sb("excess_sum", [P, CPS // 2])
        plain = sb("plain", [P, CPS // 2])
        plain_all = sb("plain_all", [P, 1])
        end_max = sb("end_max", [P, 1])
        good = sb("good", [P, 1])
        bad = sb("bad", [P, 1])
        bad_all = sb("bad_all", [P, 1])
        flag = sb("flag", [P, 1], i32)
        w1_sb = sb("w1_sb", [P, D])
        b1_sb = sb("b1_sb", [P, D])
        s_tile = sb("s_tile", [P, 1])
        top = sb("top", [P, 1])
        top_s = sb("top_s", [P, 1])
        top_l = sb("top_l", [P, 1])
        neg_top = sb("neg_top", [P, 1])
        den = sb("den", [P, 1])
        x1_tile = sb("x1_tile", [P, D])
        h2 = sb("h2", [P, D])
        h2T = sb("h2T", [P, D])

        code_words = codes[:, :, :].bitcast(fp32).rearrange("p c (k n) -> p c k n", k=KB)
        g_adj, g_score, g_weight, g_wT = (ring[:, n, :] for n in range(4))
        g_diag_d = unmasked[:, 0, 0, 0:KB * P]
        msg = aw[:, :, 0:D]

        def hn_block(b):
            return unmasked[:, b // 16, b % 16 // 4, b % 4 * P:(b % 4 + 1) * P]

        bank = [ctx.enter_context(nc.psum_tensor(f"bank{n}", [P, 512], fp32)) for n in range(8)]
        tr_bank = [bank[n][:, :].bitcast(fp8).rearrange("p (i e) -> p e i", e=GW) for n in range(TB)]

        def acc_of(h, k):
            return bank[4 + 2 * h + k // 2][:, (k % 2) * E1:(k % 2 + 1) * E1]

        w_loaded, a_loaded, diag_loaded = sem("w_loaded"), sem("a_loaded"), sem("diag_loaded")
        x_loaded = [sem(f"x_loaded{o}") for o in range(XO)]
        adj_ready = [sem(f"adj_ready{c}") for c in range(AR)]
        consts_set, ident_set = sem("consts_set"), sem("ident_set")
        w0T_done, w0T_copied, wa_done, wa_copied = (
            sem(n) for n in ("w0T_done", "w0T_copied", "wa_done", "wa_copied"))
        stats_set, moments_set, std_set, rstd_set, hn_done, hT_done, hT_copied = (
            sem(n) for n in ("stats_set", "moments_set", "std_set", "rstd_set", "hn_done", "hT_done", "hT_copied"))
        whe_done, whe_copied, whe_last_copied, s_spread, s_row_low, s_row_high, row_set = (
            sem(n) for n in ("whe_done", "whe_copied", "whe_last_copied", "s_spread", "s_row_low", "s_row_high", "row_set"))
        ends_step, ends_reduced, dmax_set, a_set, q_set, aw_set, sd_set, pair_done, self_step = (
            sem(n) for n in ("ends_step", "ends_reduced", "dmax_set", "a_set", "q_set", "aw_set", "sd_set",
                             "pair_done", "self_step"))
        end_max_set = sem("end_max_set")
        transposed, unmasked_set, masked, mm_done, coded, summed_up = (
            sem(n) for n in ("transposed", "unmasked_set", "masked", "mm_done", "coded", "summed_up"))
        summed_set, rden_set, pool_step, finished, rows_free = (
            sem(n) for n in ("summed_set", "rden_set", "pool_step", "finished", "rows_free"))
        verdict_step, bad_reduced, flag_set = sem("verdict_step"), sem("bad_reduced"), sem("flag_set")
        g_w1, g_b1, g_loaded, g_diag, g_drow, g_drow_set = (
            sem(n) for n in ("g_w1", "g_b1", "g_loaded", "g_diag", "g_drow", "g_drow_set"))
        g0_vec, g0_exp, g0_tr, g0_ev, g0_mm, g0_std, g0_h2tr, g0_h2T, g0_msg = (
            sem(n) for n in ("g0_vec", "g0_exp", "g0_tr", "g0_ev", "g0_mm", "g0_std", "g0_h2tr",
                             "g0_h2T", "g0_msg"))
        g1_loaded, g1_vec, g1_act, g1_tr, g1_ev, g1_mm, g1_row_free = (
            sem(n) for n in ("g1_loaded", "g1_vec", "g1_act", "g1_tr", "g1_ev", "g1_mm", "g1_row_free"))

        block = ctx.enter_context(nc.Block())

        @block.sync
        def _(sp):
            sp.dma_start(w0_sb[:, 0:D], w0).then_inc(w_loaded, 16)
            with nc.allow_non_contiguous_dma(reason="256 values"):
                sp.dma_start(a_sb[:, :], a0.rearrange("(c d) -> d c", c=2)).then_inc(a_loaded, 16)

            def load_chunk(s, idx):
                half = s * 2 + idx % 2
                sp.dma_start(ring[:, idx % AR, :].rearrange("p (k n) -> p k n", k=KB),
                             adj_chunks[half, idx // 2]).then_inc(adj_ready[idx % AR], 16)

            def load_into_used_slot(s, idx):
                sp.wait_ge(summed_up, s * CPS + idx - AR + 1)
                load_chunk(s, idx)

            sp.nop().then_inc(rows_free, 2 * 16)

            def store(s, h):
                half = s * 2 + h
                sp.wait_ge(finished, half + 1)
                sp.dma_start(out_halves[half], summed[:, h, :, 0:D]).then_inc(rows_free, 16)

            for o in range(XO):
                sp.dma_start(x_sb[:, o * BPO:(o + 1) * BPO, :], x_octants[o]).then_inc(x_loaded[o], 16)
            load_chunk(0, 0)
            with nc.allow_non_contiguous_dma(reason="4096 values"):
                for k in range(KB):
                    sp.dma_start(diag[:, :].rearrange("p (s k) -> p k s", k=KB)[:, k, :],
                                 adj_diagonal[k]).then_inc(diag_loaded, 16)
            for idx in range(1, AR):
                load_chunk(0, idx)
            for idx in range(AR, CPS):
                load_into_used_slot(0, idx)
            with sp.Fori(1, NS) as s:
                for idx in range(CPS):
                    load_into_used_slot(s, idx)
                for h in range(2):
                    store(s - 1, h)
            for h in range(2):
                store(NS - 1, h)
            sp.wait_ge(rows_free, 16 * (NH + 2))

            sp.wait_ge(flag_set, 1)
            general = sp.value_load(flag[0:1, 0:1])
            with sp.If(general != 0):
                sp.dma_start(w1_sb[:, :], w1).then_inc(g_w1, 16)
                sp.dma_start(b1_sb[:, :], b1.partition_broadcast(P)).then_inc(g_b1, 16)

                def load_row_tile(sup, k):
                    if not (isinstance(sup, int) and sup + k == 0):
                        sp.wait_ge(g0_vec, G0_STEPS * (sup * KB + k - 1) + 1)
                    sp.dma_start(g_adj, adj_tiles[sup, k]).then_inc(g_loaded, 16)

                def store_and_load(sup, k, before):
                    sp.wait_ge(g1_vec, G1_STEPS * (sup * KB + k))
                    sp.dma_start(out_tiles[before], summed[:, 0, 0, 0:D]).then_inc(g1_row_free, 16)
                    sp.dma_start(g_adj, adj_tiles[sup, k]).then_inc(g1_loaded, 16)

                for k in range(KB):
                    load_row_tile(0, k)
                with sp.Fori(1, NH) as sup:
                    for k in range(KB):
                        load_row_tile(sup, k)
                sp.nop().then_inc(g1_row_free, 16)
                sp.wait_ge(g0_vec, G0_STEPS * (NB - 1) + 1)
                sp.dma_start(g_adj, adj_tiles[0, 0]).then_inc(g1_loaded, 16)
                for k in range(1, KB):
                    store_and_load(0, k, (0, k - 1))
                with sp.Fori(1, NH) as sup:
                    store_and_load(sup, 0, (sup - 1, KB - 1))
                    for k in range(1, KB):
                        store_and_load(sup, k, (sup, k - 1))
                sp.wait_ge(g1_vec, G1_STEPS * NB)
                sp.dma_start(out_tiles[NH - 1, KB - 1], summed[:, 0, 0, 0:D]).then_inc(g1_row_free, 16)
                sp.wait_ge(g1_row_free, 16 * (NB + 1))

        @block.gpsimd
        def _(pool):
            nc.gpsimd.memset(ident[:, :], 0.0).then_inc(consts_set, 1)
            nc.gpsimd.memset(offdiag[:, :], 1.0).then_inc(consts_set, 1)
            nc.gpsimd.memset(ones[:, :], 1.0).then_inc(consts_set, 1)
            nc.gpsimd.memset(eps_t[:, :], EPS).then_inc(consts_set, 1)
            nc.gpsimd.memset(below_one[:, :], BELOW_ONE).then_inc(consts_set, 1)
            nc.gpsimd.memset(minus_one[:, :], -1.0).then_inc(consts_set, 1)
            nc.gpsimd.memset(entries[:, :], float(KB * CW)).then_inc(consts_set, 1)
            nc.gpsimd.memset(excess_sum[:, :], 0.0).then_inc(consts_set, 1)
            pool.wait_ge(consts_set, 8)
            for tile, fill in ((ident, 1.0), (offdiag, 0.0)):
                nc.gpsimd.affine_select(out=tile[:, :], in_=tile[:, :], compare_op=ALU.not_equal, fill=fill,
                                        base=0, pattern=[[-1, P]], channel_multiplier=1).then_inc(ident_set, 1)
            pool.wait_ge(ends_step, 4)
            nc.gpsimd.partition_all_reduce(ends_all[:, :], ends[:, :], P,
                                           REDUCE_MAX).then_inc(ends_reduced, 1)
            pool.wait_ge(a_set, 1)
            for q in range(AQ):
                quarter = slice(q * BPQ, (q + 1) * BPQ)
                nc.gpsimd.tensor_tensor(aw[:, quarter, 0:D], whe[:, quarter, 0:D],
                                        aw[:, quarter, D:D + 1].broadcast_to([P, BPQ, D]), ALU.mult).then_inc(aw_set, 1)

            def tally(s, part):
                done = part * (CPS // 2)
                chunks = slice(done, done + CPS // 2)
                pool.wait_ge(summed_up, s * CPS + done + CPS // 2)
                nc.gpsimd.tensor_tensor(excess[:, part, :], sizes[:, chunks], sizes[:, chunks],
                                        ALU.add).then_inc(pool_step, 1)
                pool.wait_ge(pool_step, s * POOL_STEPS + 4 * part + 1)
                pool.wait_ge(coded, s * CPS + done + CPS // 2)
                nc.gpsimd.tensor_tensor(excess[:, part, :], excess[:, part, :], signs[:, chunks],
                                        ALU.add).then_inc(pool_step, 1)
                pool.wait_ge(pool_step, s * POOL_STEPS + 4 * part + 2)
                nc.gpsimd.tensor_tensor(excess[:, part, :], excess[:, part, :], entries[:, :],
                                        ALU.subtract).then_inc(pool_step, 1)
                pool.wait_ge(pool_step, s * POOL_STEPS + 4 * part + 3)
                nc.gpsimd.tensor_tensor(excess[:, part, :], excess[:, part, :], excess[:, part, :],
                                        ALU.mult).then_inc(pool_step, 1)

            def add_up(part):
                nc.gpsimd.tensor_tensor(excess_sum[:, :], excess_sum[:, :], excess[:, part, :],
                                        ALU.add).then_inc(pool_step, 1)

            def output_rows(s, h):
                pool.wait_ge(rden_set, s * 2 + h + 1)
                nc.gpsimd.tensor_tensor(summed[:, h, :, 0:D], summed[:, h, :, 0:D],
                                        rden[:, h, :].rearrange("p (k o) -> p k o", o=1).broadcast_to([P, KB, D]),
                                        ALU.mult).then_inc(pool_step, 1)
                pool.wait_ge(pool_step, s * POOL_STEPS + 9 + 2 * h)
                add_up(h)
                nc.gpsimd.tensor_tensor(summed[:, h, :, 0:D], summed[:, h, :, 0:D],
                                        x_sb[:, bass.ds((s * 2 + h) * KB, KB), :], ALU.add).then_inc(finished, 1)

            with pool.Fori(0, NS - 1) as s:
                tally(s, 0)
                tally(s, 1)
                output_rows(s, 0)
                output_rows(s, 1)
            tally(NS - 1, 0)
            tally(NS - 1, 1)
            for part in range(2):
                pool.wait_ge(pool_step, (NS - 1) * POOL_STEPS + 8 + part)
                add_up(part)
            pool.wait_ge(verdict_step, 4)
            nc.gpsimd.partition_all_reduce(bad_all[:, :], bad[:, :], P,
                                           REDUCE_MAX).then_inc(bad_reduced, 1)

        @block.tensor
        def _(pe):
            pe.wait_ge(ident_set, 2)
            pe.wait_ge(w_loaded, 16)
            nc.tensor.transpose(bank[7][:, 0:D], w0_sb[:, 0:D], ident[:, :]).then_inc(w0T_done, 1)
            pe.wait_ge(w0T_copied, 1)
            pe.wait_ge(a_loaded, 16)
            nc.tensor.matmul(bank[6][:, 0:2], w0T[:, :], a_sb[:, :], start=True, stop=True).then_inc(wa_done, 1)

            def transpose_h(n):
                pe.wait_ge(hn_done, n + 1)
                if n >= 2:
                    pe.wait_ge(hT_copied, n - 1)
                for b in range(4):
                    last = nc.tensor.transpose(bank[n % 2][:, b * P:(b + 1) * P],
                                               hn_block(4 * n + b), ident[:, :])
                last.then_inc(hT_done, 1)

            def project(n):
                pe.wait_ge(hT_copied, n + 1)
                for half in range(2):
                    if n >= 1:
                        pe.wait_ge(whe_copied, 2 * n - 1 + half)
                    for b in range(2):
                        nb = 4 * n + 2 * half + b
                        last = nc.tensor.matmul(bank[2 + half][:, b * E2:(b + 1) * E2], hT[:, nb * P:(nb + 1) * P],
                                                w0_sb[:, :], start=(b == 0), stop=(b == 1), skip_group_check=True)
                    last.then_inc(whe_done, 1)

            def spread_s(n):
                if n + 1 < NB // 4:
                    pe.wait_ge(whe_copied, 2 * n + 2)
                else:
                    pe.wait_ge(whe_last_copied, 2)
                if n >= 4:
                    pe.wait_ge(s_row_low, n - 3)
                for b in range(4):
                    last = nc.tensor.transpose(bank[4 + n % 4][:, b * P:(b + 1) * P],
                                               whe[:, 4 * n + b, D:D + 1].broadcast_to([P, P]), ident[:, :])
                last.then_inc(s_spread, 1)

            transpose_h(0)
            pe.wait_ge(wa_copied, 1)
            for n in range(NB // 4):
                if n + 1 < NB // 4:
                    transpose_h(n + 1)
                if n >= 1 and n + 1 < NB // 4:
                    spread_s(n - 1)
                project(n)
            spread_s(NB // 4 - 2)
            spread_s(NB // 4 - 1)
            pe.wait_ge(hT_copied, NB // 4)
            pe.wait_ge(whe_last_copied, 2)
            pe.wait_ge(s_row_high, 4)

            def transpose_unit(s, u, first):
                idx, part = u // 4 * 2 + u % 2, u // 2 % 2
                if part == 0:
                    pe.wait_ge(coded, s * CPS + idx + 1)
                if not first or u >= TB:
                    pe.wait_ge(masked, s * UPS + u - TB + 1)
                for k in range(KB):
                    last = nc.tensor.transpose(bank[u % TB][:, k * P:(k + 1) * P],
                                               code_words[:, idx % CR, k, part * P:(part + 1) * P], ident[:, :])
                last.then_inc(transposed, 1)

            def multiply_unit(s, u, first, blocks=range(GW)):
                g, h = u // 2, u % 2
                if g == 0 and not first:
                    pe.wait_ge(summed_set, s * 2 - 1 + h)
                pe.wait_ge(masked, s * UPS + u + 1)
                for e in blocks:
                    jb = GW * g + e
                    if first and h == 0 and jb % BPQ == 0:
                        pe.wait_ge(aw_set, jb // BPQ + 1)
                    for k in range(KB):
                        last = nc.tensor.matmul(acc_of(h, k),
                                                weights[u % WR][:, e * HR + k * P:e * HR + (k + 1) * P],
                                                aw[:, jb, :], start=(jb == 0 and k % 2 == 0), stop=(jb == NB - 1),
                                                skip_group_check=True)
                if e == GW - 1:
                    last.then_inc(mm_done, 1)

            def supertile(s, first, last):
                for u in range(1 if first else 0, UPS):
                    if u + 2 < UPS:
                        transpose_unit(s, u + 2, first)
                    elif not last:
                        transpose_unit(s + 1, u + 2 - UPS, False)
                    multiply_unit(s, u, first)

            transpose_unit(0, 0, True)
            multiply_unit(0, 0, True, range(1))
            transpose_unit(0, 1, True)
            multiply_unit(0, 0, True, range(1, GW))
            transpose_unit(0, 2, True)
            supertile(0, True, False)
            with pe.Fori(1, NS - 1) as s:
                supertile(s, False, False)
            supertile(NS - 1, False, True)

            def general_transposes(tr, ev, t):
                for n in range(8):
                    if n >= 4:
                        pe.wait_ge(ev, t * 8 + n - 3)
                    for b in range(4):
                        jb = 4 * n + b
                        last = nc.tensor.transpose(bank[n % 4][:, b * P:(b + 1) * P],
                                                   g_weight[:, jb * P:(jb + 1) * P], ident[:, :])
                    last.then_inc(tr, 1)

            pe.wait_ge(flag_set, 1)
            general = pe.value_load(flag[0:1, 0:1])
            with pe.If(general != 0):
                for n in range(8):
                    pe.wait_ge(g_diag, n + 1)
                    if n >= 2:
                        pe.wait_ge(g_drow_set, n - 1)
                    nc.tensor.matmul(bank[n % 2][:, :], ones[:, :], g_diag_d, start=True, stop=True).then_inc(g_drow, 1)
                pe.wait_ge(g_drow_set, 8)
                pe.wait_ge(g_w1, 16)
                with pe.Fori(0, NB) as t:
                    pe.wait_ge(g0_exp, t + 1)
                    general_transposes(g0_tr, g0_ev, t)
                    pe.wait_ge(g0_ev, t * 8 + 8)
                    for jb in range(NB):
                        last = nc.tensor.matmul(bank[4][:, 0:D], g_wT[:, jb * P:(jb + 1) * P], whe[:, jb, 0:D],
                                                start=(jb == 0), stop=(jb == NB - 1))
                    last.then_inc(g0_mm, 1)
                    pe.wait_ge(g0_vec, G0_STEPS * t + G0_STEPS - 1)
                    nc.tensor.transpose(bank[5][:, 0:P], h2[:, :], ident[:, :]).then_inc(g0_h2tr, 1)
                    pe.wait_ge(g0_h2T, t + 1)
                    nc.tensor.matmul(bank[6][:, 0:D], h2T[:, :], w1_sb[:, :],
                                     start=True, stop=True).then_inc(g0_msg, 1)
                pe.wait_ge(g0_vec, G0_STEPS * NB)
                with pe.Fori(0, NB) as t:
                    pe.wait_ge(g1_vec, G1_STEPS * t + 5)
                    general_transposes(g1_tr, g1_ev, t)
                    pe.wait_ge(g1_ev, t * 8 + 8)
                    for jb in range(NB):
                        last = nc.tensor.matmul(bank[4][:, 0:D], g_wT[:, jb * P:(jb + 1) * P], msg[:, jb, :],
                                                start=(jb == 0), stop=(jb == NB - 1))
                    last.then_inc(g1_mm, 1)

        @block.scalar
        def _(act):
            act.wait_ge(consts_set, 8)

            def deviations(o):
                octant = slice(o * BPO, (o + 1) * BPO)
                act.wait_ge(moments_set, o + 1)
                nc.scalar.activation(std[:, octant], mv[:, octant, 1], ACT.Sqrt,
                                     bias=eps_t[:, :]).then_inc(std_set, 1)

            def rectify(n):
                act.wait_ge(hT_done, n + 1)
                nc.scalar.activation(hT[:, n * 512:(n + 1) * 512], bank[n % 2][:, :],
                                     ACT.Relu).then_inc(hT_copied, 1)

            def s_row(n):
                act.wait_ge(s_spread, n + 1)
                nc.scalar.activation(row[:, n * 512:(n + 1) * 512], bank[4 + n][:, :],
                                     ACT.Copy).then_inc(s_row_low, 1)

            def q_of_blocks(blocks):
                nc.scalar.activation(q_col[:, blocks], whe[:, blocks, D + 1], ACT.Exp,
                                     scale=-(1 - SLOPE)).then_inc(q_set, 1)

            def r_row(nodes):
                nc.scalar.activation(row[:, nodes], row[:, nodes], ACT.Exp, scale=-(1 - SLOPE)).then_inc(row_set, 1)

            def await_chunk(s, idx, first):
                act.wait_ge(adj_ready[idx % AR], (s * 2 + idx // AR + 1) * 16)
                if not first or idx >= CR:
                    act.wait_ge(transposed, s * UPS + idx // 2 * 4 + idx % 2 - 5)
                if idx == 0 and not first:
                    act.wait_ge(pool_step, s * POOL_STEPS - POOL_STEPS + 2)
                if idx == CPS // 2 and not first:
                    act.wait_ge(pool_step, s * POOL_STEPS - POOL_STEPS + 6)

            def code_entries(idx):
                nc.scalar.activation(codes[:, idx % CR], ring[:, idx % AR, :], ACT.Sign, bias=below_one[:, :], scale=-1.0,
                                     accum_out=signs[:, idx:idx + 1], saturate=False).then_inc(coded, 1)

            def sum_entries(idx):
                nc.scalar.activation(ring[:, idx % AR, :], ring[:, idx % AR, :], ACT.Abs,
                                     accum_out=sizes[:, idx:idx + 1]).then_inc(summed_up, 1)

            def supertile(s, first, last):
                for idx in range(CPS):
                    if first and idx < 2:
                        sum_entries(idx)
                        if idx == 0:
                            await_chunk(0, 3, True)
                            code_entries(3)
                        continue
                    if idx + 2 < CPS:
                        await_chunk(s, idx + 2, first)
                    elif not last:
                        await_chunk(s + 1, idx + 2 - CPS, False)
                    sum_entries(idx)
                    if idx + 2 < CPS or not last:
                        code_entries((idx + 2) % CPS)
                    if first and 4 <= idx < 4 + NS - 1:
                        if idx == 4:
                            act.wait_ge(s_row_low, 4)
                            act.wait_ge(s_row_high, 4)
                        r_row(slice((idx - 3) * 2 * HR, (idx - 2) * 2 * HR))

            def copy_projection(n):
                for half in range(2):
                    act.wait_ge(whe_done, 2 * n + half + 1)
                    nb = 4 * n + 2 * half
                    nc.scalar.activation(whe[:, nb:nb + 2, :],
                                         bank[2 + half][:, 0:2 * E2].rearrange("p (b n) -> p b n", b=2),
                                         ACT.Copy).then_inc(whe_copied, 1)

            for o in range(MOMENTS_AHEAD):
                deviations(o)
            rectify(0)
            for n in range(NB // 4 - 1):
                if n + MOMENTS_AHEAD < XO:
                    deviations(n + MOMENTS_AHEAD)
                rectify(n + 1)
                if 1 <= n <= 4:
                    s_row(n - 1)
                copy_projection(n)
            act.wait_ge(s_row_low, 2)
            r_row(slice(0, 2 * HR))
            q_of_blocks(slice(0, BPQ))
            act.wait_ge(whe_copied, NB // 2 - 2)
            act.wait_ge(whe_last_copied, 2)
            q_of_blocks(slice(BPQ, NB))
            await_chunk(0, 0, True)
            code_entries(0)
            act.wait_ge(dmax_set, 1)
            nc.scalar.activation(aw[:, :, D], whe[:, :, D + 1], ACT.Exp, bias=neg_dmax[:, :]).then_inc(a_set, 1)
            await_chunk(0, 1, True)
            code_entries(1)
            act.wait_ge(sd_set, 1)
            nc.scalar.activation(pair_ii[:, :], sd_sum[:, :], ACT.Exp, scale=-(1 - SLOPE)).then_inc(pair_done, 1)

            await_chunk(0, 2, True)
            code_entries(2)
            supertile(0, True, False)
            with act.Fori(1, NS - 1) as s:
                supertile(s, False, False)
            supertile(NS - 1, False, True)

            def general_copies(tr, ev, t):
                for n in range(8):
                    act.wait_ge(tr, t * 8 + n + 1)
                    nc.scalar.activation(g_wT[:, n * 512:(n + 1) * 512], bank[n % 4][:, :],
                                         ACT.Copy).then_inc(ev, 1)

            act.wait_ge(flag_set, 1)
            general = act.value_load(flag[0:1, 0:1])
            with act.If(general != 0):
                for n in range(8):
                    act.wait_ge(g_drow, n + 1)
                    nc.scalar.activation(row[:, n * 512:(n + 1) * 512], bank[n % 2][:, :],
                                         ACT.Copy).then_inc(g_drow_set, 1)
                with act.Fori(0, NB) as t:
                    act.wait_ge(g0_vec, G0_STEPS * t + 10)
                    nc.scalar.activation(g_weight, g_score, ACT.Exp, bias=neg_top[:, :],
                                         accum_out=den[:, :]).then_inc(g0_exp, 1)
                    general_copies(g0_tr, g0_ev, t)
                    act.wait_ge(g0_vec, G0_STEPS * t + 15)
                    nc.scalar.activation(std[:, 0:1], mv[:, 0, 1:2], ACT.Sqrt,
                                         bias=eps_t[:, :]).then_inc(g0_std, 1)
                    act.wait_ge(g0_h2tr, t + 1)
                    nc.scalar.activation(h2T[:, :], bank[5][:, 0:P], ACT.Relu).then_inc(g0_h2T, 1)
                with act.Fori(0, NB) as t:
                    act.wait_ge(g1_vec, G1_STEPS * t + 4)
                    nc.scalar.activation(g_weight, g_score, ACT.Square, bias=minus_one[:, :]).then_inc(g1_act, 1)
                    act.wait_ge(g1_act, t * 2 + 1)
                    nc.scalar.activation(g_score, g_weight, ACT.Exp, scale=-2.0).then_inc(g1_act, 1)
                    general_copies(g1_tr, g1_ev, t)

        @block.vector
        def _(dve):
            dve.wait_ge(consts_set, 8)
            dve.wait_ge(w0T_done, 1)
            nc.vector.tensor_copy(w0T[:, :], bank[7][:, 0:D]).then_inc(w0T_copied, 1)

            def moments(o):
                blocks = range(o * BPO, (o + 1) * BPO)
                dve.wait_ge(x_loaded[o], 16)
                for b in blocks:
                    last = nc.vector.bn_stats(stats[:, b, :], x_sb[:, b, :])
                last.then_inc(stats_set, 1)
                dve.wait_ge(stats_set, o + 1)
                for b in blocks:
                    last = nc.vector.bn_aggr(mv[:, b, :], stats[:, b, :])
                last.then_inc(moments_set, 1)

            def normalise(o):
                octant = slice(o * BPO, (o + 1) * BPO)
                dve.wait_ge(std_set, o + 1)
                nc.vector.reciprocal(rstd[:, octant], std[:, octant]).then_inc(rstd_set, 1)
                dve.wait_ge(rstd_set, o + 1)
                for b in range(o * BPO, (o + 1) * BPO):
                    last = nc.vector.tensor_scalar(hn_block(b), x_sb[:, b, :], mv[:, b, 0:1], rstd[:, b:b + 1],
                                                   ALU.subtract, ALU.mult)
                last.then_inc(hn_done, 1)

            moments(0)
            dve.wait_ge(wa_done, 1)
            nc.vector.tensor_copy(w0_sb[:, D:D + 2], bank[6][:, 0:2]).then_inc(wa_copied, 1)
            for o in range(1, MOMENTS_AHEAD):
                moments(o)
            for o in range(XO):
                normalise(o)
                if o + MOMENTS_AHEAD < XO:
                    moments(o + MOMENTS_AHEAD)

            def self_edges():
                dve.wait_ge(pair_done, 1)
                nc.vector.tensor_scalar(w_self[:, :], pair_ii[:, :], 1.0, None, ALU.max).then_inc(self_step, 1)
                dve.wait_ge(self_step, 1)
                dve.wait_ge(diag_loaded, 16 * KB)
                nc.vector.scalar_tensor_tensor(w_diag[:, :], diag[:, :], 0.0, w_self[:, :],
                                               ALU.is_le, ALU.mult).then_inc(self_step, 1)
                dve.wait_ge(self_step, 2)

            def unmask_columns(s, g, e):
                jb = GW * g + e
                return nc.vector.tensor_scalar(unmasked[:, g % MR, e, :], row[:, bass.ds(s * (2 * HR), 2 * HR)],
                                               q_col[:, jb:jb + 1], 1.0, ALU.mult, ALU.max)

            def await_unmasked_slot(s, g, first):
                if not first or g >= MR:
                    dve.wait_ge(masked, s * UPS + 2 * (g - MR + 1))

            def await_unit(s, u, first):
                dve.wait_ge(transposed, s * UPS + u + 1)
                dve.wait_ge(unmasked_set, s * GPS + u // 2 + 1)
                if not first or u >= WR:
                    dve.wait_ge(mm_done, s * UPS + u - WR + 1)

            def mask_unit(u):
                g, h = u // 2, u % 2
                nc.vector.scalar_tensor_tensor(weights[u % WR].rearrange("p (e i) -> p e i", e=GW), tr_bank[u % TB],
                                               0.0, unmasked[:, g % MR, :, h * HR:(h + 1) * HR],
                                               ALU.is_lt, ALU.mult).then_inc(masked, 1)

            def finish_half(s, h, first):
                half = s * 2 + h
                dve.wait_ge(mm_done, s * UPS + UPS - 1 + h)
                if not first:
                    dve.wait_ge(rows_free, (s + 1) * 32)
                for k in range(KB):
                    last = nc.vector.scalar_tensor_tensor(summed[:, h, k, :], aw[:, bass.ds(half * KB + k, 1), :],
                                                          w_diag[:, bass.ds(half * KB + k, 1)], acc_of(h, k),
                                                          ALU.mult, ALU.add)
                last.then_inc(summed_set, 1)
                dve.wait_ge(summed_set, half + 1)
                nc.vector.reciprocal(rden[:, h, :], summed[:, h, :, D]).then_inc(rden_set, 1)

            def judge():
                def verdict(ins, n):
                    ins.then_inc(verdict_step, 1)
                    dve.wait_ge(verdict_step, n)

                dve.wait_ge(pool_step, (NS - 1) * POOL_STEPS + 10)
                verdict(nc.vector.tensor_scalar(plain[:, :], excess_sum[:, :], 0.0, None, ALU.is_equal), 1)
                verdict(nc.vector.tensor_reduce(plain_all[:, :], plain[:, :], AX.X, ALU.min), 2)
                dve.wait_ge(end_max_set, 1)
                verdict(nc.vector.tensor_scalar(good[:, :], end_max[:, :], RANGE, plain_all[:, :],
                                                ALU.is_le, ALU.mult), 3)
                verdict(nc.vector.tensor_scalar(bad[:, :], good[:, :], -1.0, 1.0, ALU.mult, ALU.add), 4)
                dve.wait_ge(bad_reduced, 1)
                nc.vector.tensor_copy(flag[:, :], bad_all[:, :]).then_inc(flag_set, 1)

            def supertile(s, first, last):
                for u in range(UPS):
                    g, h = u // 2, u % 2
                    if g + 1 < GPS or not last:
                        ahead = (s, g + 1) if g + 1 < GPS else (s + 1, 0)
                        if h == 0:
                            await_unmasked_slot(*ahead, first and g + 1 < GPS)
                            if first and g + 1 == GPS:
                                dve.wait_ge(row_set, NS)
                        if first and u == 0:
                            await_unit(s, u, first)
                            mask_unit(u)
                            unmask_columns(*ahead, 0)
                            unmask_columns(*ahead, 1)
                        elif first:
                            unmask_columns(*ahead, 2 * h)
                            quarter = unmask_columns(*ahead, 2 * h + 1)
                            if h == 1:
                                quarter.then_inc(unmasked_set, 1)
                            await_unit(s, u, first)
                            mask_unit(u)
                            if u == 2:
                                self_edges()
                        elif u == 1:
                            await_unit(s, u, first)
                            unmask_columns(*ahead, 2)
                            mask_unit(u)
                            finish_half(s - 1, 1, first=False)
                            unmask_columns(*ahead, 3).then_inc(unmasked_set, 1)
                        else:
                            unmask_columns(*ahead, 2 * h)
                            await_unit(s, u, first)
                            quarter = unmask_columns(*ahead, 2 * h + 1)
                            if h == 1:
                                quarter.then_inc(unmasked_set, 1)
                            mask_unit(u)
                            if u == 0:
                                finish_half(s - 1, 0, first=False)
                    else:
                        await_unit(s, u, first)
                        mask_unit(u)
                if last:
                    judge()
                    for h in range(2):
                        finish_half(s, h, first=False)
                        dve.wait_ge(rden_set, s * 2 + h + 1)
                        for k in range(KB):
                            rows = nc.vector.scalar_tensor_tensor(summed[:, h, k, 0:D], summed[:, h, k, 0:D],
                                                                  rden[:, h, k:k + 1],
                                                                  x_sb[:, (s * 2 + h) * KB + k, :],
                                                                  ALU.mult, ALU.add)
                        rows.then_inc(finished, 1)

            def s_row(n):
                dve.wait_ge(s_spread, n + 1)
                nc.vector.tensor_copy(row[:, n * 512:(n + 1) * 512], bank[n][:, :]).then_inc(s_row_high, 1)

            s_row(4)
            s_row(5)
            for half in range(2):
                dve.wait_ge(whe_done, NB // 2 - 1 + half)
                nb = NB - 4 + 2 * half
                nc.vector.tensor_copy(whe[:, nb:nb + 2, :],
                                      bank[2 + half][:, 0:2 * E2].rearrange("p (b n) -> p b n", b=2)).then_inc(whe_last_copied, 1)
            s_row(6)
            dve.wait_ge(q_set, 1)
            dve.wait_ge(row_set, 1)
            dve.wait_ge(hT_done, NB // 4)
            unmask_columns(0, 0, 0)
            dve.wait_ge(whe_copied, NB // 2 - 2)
            dve.wait_ge(whe_last_copied, 2)
            for n, (col, op, neg) in enumerate(((D + 1, ALU.max, False), (D + 1, ALU.min, True),
                                                (D, ALU.max, False), (D, ALU.min, True))):
                nc.vector.tensor_reduce(ends[:, n:n + 1], whe[:, :, col], AX.X, op, negate=neg).then_inc(ends_step, 1)
            nc.vector.tensor_tensor(sd_sum[:, :], whe[:, :, D], whe[:, :, D + 1], ALU.add).then_inc(sd_set, 1)
            s_row(7)
            unmask_columns(0, 0, 1)
            dve.wait_ge(ends_reduced, 1)
            nc.vector.tensor_scalar(neg_dmax[:, :], ends_all[:, 0:1], -1.0, None, ALU.mult).then_inc(dmax_set, 1)
            nc.vector.tensor_reduce(end_max[:, :], ends_all[:, :], AX.X, ALU.max).then_inc(end_max_set, 1)
            unmask_columns(0, 0, 2)
            unmask_columns(0, 0, 3).then_inc(unmasked_set, 1)
            dve.wait_ge(q_set, 2)
            supertile(0, True, False)
            with dve.Fori(1, NS - 1) as s:
                supertile(s, False, False)
            supertile(NS - 1, False, True)

            dve.wait_ge(flag_set, 1)
            general = dve.value_load(flag[0:1, 0:1])
            with dve.If(general != 0):
                for n in range(8):
                    if n >= 1:
                        dve.wait_ge(g_drow, n)
                    nc.vector.tensor_tensor(g_diag_d.rearrange("p (k i) -> p k i", k=KB),
                                            ident[:, :].rearrange("p (o i) -> p o i", o=1).broadcast_to([P, KB, P]),
                                            whe[:, KB * n:KB * (n + 1), D + 1:E2].broadcast_to([P, KB, P]),
                                            ALU.mult).then_inc(g_diag, 1)
                dve.wait_ge(g_drow_set, 8)
                dve.wait_ge(g_b1, 16)
                with dve.Fori(0, NB) as t:
                    def step(ins, n):
                        ins.then_inc(g0_vec, 1)
                        dve.wait_ge(g0_vec, G0_STEPS * t + n)

                    dve.wait_ge(g_loaded, t * 16 + 16)
                    step(nc.vector.tensor_scalar(g_score.rearrange("p (s k q) -> p s q k", s=NH, k=KB),
                                                 g_adj.rearrange("p (s q k) -> p s q k", s=NH, k=KB),
                                                 0.0, MASKED, ALU.is_le, ALU.mult), 1)
                    own = g_score[:, bass.ds(t * P, P)]
                    step(nc.vector.tensor_tensor(own, own, offdiag[:, :], ALU.mult), 2)
                    step(nc.vector.tensor_tensor(g_score, g_score, row[:, :], ALU.add), 3)
                    step(nc.vector.tensor_scalar(s_tile[:, :], whe[:, bass.ds(t, 1), D], 1.0, None, ALU.mult), 4)
                    step(nc.vector.tensor_reduce(top[:, :], g_score, AX.X, ALU.max), 5)
                    step(nc.vector.tensor_scalar(g_score, g_score, s_tile[:, :], None, ALU.add), 6)
                    step(nc.vector.scalar_tensor_tensor(g_score, g_score, SLOPE, g_score, ALU.mult, ALU.max), 7)
                    step(nc.vector.tensor_tensor(top_s[:, :], top[:, :], s_tile[:, :], ALU.add), 8)
                    step(nc.vector.scalar_tensor_tensor(top_l[:, :], top_s[:, :], SLOPE, top_s[:, :],
                                                        ALU.mult, ALU.max), 9)
                    step(nc.vector.tensor_scalar(neg_top[:, :], top_l[:, :], -1.0, None, ALU.mult), 10)
                    dve.wait_ge(g0_exp, t + 1)
                    step(nc.vector.reciprocal(rden[:, 0, 0:1], den[:, :]), 11)
                    dve.wait_ge(g0_mm, t + 1)
                    step(nc.vector.scalar_tensor_tensor(x1_tile[:, :], bank[4][:, 0:D], rden[:, 0, 0:1],
                                                        x_sb[:, bass.ds(t, 1), :], ALU.mult, ALU.add), 12)
                    step(nc.vector.bn_stats(stats[:, 0, :], x1_tile[:, :]), 13)
                    nc.vector.tensor_scalar(x_sb[:, bass.ds(t, 1), :], x1_tile[:, :], 1.0, None, ALU.mult).then_inc(g0_vec, 1)
                    step(nc.vector.bn_aggr(mv[:, 0, :], stats[:, 0, :]), 15)
                    dve.wait_ge(g0_std, t + 1)
                    step(nc.vector.reciprocal(rstd[:, 0:1], std[:, 0:1]), 16)
                    step(nc.vector.tensor_scalar(h2[:, :], x1_tile[:, :], mv[:, 0, 0:1], rstd[:, 0:1],
                                                 ALU.subtract, ALU.mult), 17)
                    dve.wait_ge(g0_msg, t + 1)
                    step(nc.vector.tensor_tensor(msg[:, bass.ds(t, 1), :], bank[6][:, 0:D], b1_sb[:, :], ALU.add), 18)
                with dve.Fori(0, NB) as t:
                    def step(ins, n):
                        ins.then_inc(g1_vec, 1)
                        dve.wait_ge(g1_vec, G1_STEPS * t + n)

                    dve.wait_ge(g1_loaded, t * 16 + 16)
                    step(nc.vector.tensor_scalar(g_wT, g_adj, 0.0, TINY, ALU.is_equal, ALU.mult), 1)
                    step(nc.vector.tensor_tensor(g_weight, g_adj, g_wT, ALU.add), 2)
                    step(nc.vector.reciprocal(g_wT, g_weight), 3)
                    step(nc.vector.tensor_scalar(g_score.rearrange("p (s k q) -> p s q k", s=NH, k=KB),
                                                 g_wT.rearrange("p (s q k) -> p s q k", s=NH, k=KB),
                                                 RECIPROCAL_MAX, -RECIPROCAL_MAX, ALU.min, ALU.max), 4)
                    dve.wait_ge(g1_act, t * 2 + 2)
                    for c in range(NH):
                        columns = slice(c * HR, (c + 1) * HR)
                        last = nc.vector.scalar_tensor_tensor(
                            g_weight[:, columns].rearrange("p (k q) -> p k q", k=KB),
                            g_adj[:, columns].rearrange("p (q k) -> p k q", k=KB), 1.0,
                            g_score[:, columns].rearrange("p (k q) -> p k q", k=KB), ALU.is_lt, ALU.mult)
                    step(last, 5)
                    dve.wait_ge(g1_mm, t + 1)
                    dve.wait_ge(g1_row_free, t * 16 + 16)
                    step(nc.vector.tensor_tensor(summed[:, 0, 0, 0:D], bank[4][:, 0:D], x_sb[:, bass.ds(t, 1), :],
                                                 ALU.add), 6)


_INS = ["x", "adj", "L0_gnn_W", "L0_gnn_a", "L1_gnn_W", "L1_gnn_B"]


def kernel(**inputs):
    import numpy as np
    import concourse.bacc as bacc
    from concourse.bass_utils import run_bass_kernel_spmd

    nc = bacc.Bacc("TRN2", target_bir_lowering=False, num_devices=1)
    arrays, args = {}, []
    for name in _INS:
        a = np.ascontiguousarray(inputs[name])
        arrays[f"in_{name}"] = a
        args.append(nc.dram_tensor(f"in_{name}", a.shape, mybir.dt.from_np(a.dtype), kind="ExternalInput").ap())
    args.append(nc.dram_tensor("out_0", (N, D), mybir.dt.float32, kind="ExternalOutput").ap())
    gnn_program(nc, *args)
    return run_bass_kernel_spmd(nc, [arrays], core_ids=[0]).results[0]["out_0"]
```
